# Optimizing a Trainium2 kernel written in Bass

```python
import numpy as np
import jax
import jax.numpy as jnp

def _softmax(x, axis=-1):
    return jax.nn.softmax(x, axis=axis)

def _gelu(x):
    return jax.nn.gelu(x, approximate=True)

def _silu(x):
    return jax.nn.silu(x)

def _sigmoid(x):
    return jax.nn.sigmoid(x)

def _layernorm(x, axis=-1, eps=1e-05):
    m = jnp.mean(x, axis=axis, keepdims=True)
    v = jnp.var(x, axis=axis, keepdims=True)
    return (x - m) / jnp.sqrt(v + eps)

def _scatter_add(tgt, idx, src, axis=0):
    return tgt.at[idx].add(src)

def _segment_sum(src, seg, n):
    return jax.ops.segment_sum(src, seg, n)
kernel_name = 'mk_gnn_resnorm_d2_gnn_r8_eefc10'

def setup_inputs(seed: int=0):
    np.random.seed(seed)
    _w = jnp.asarray

    def _rec_inputs():
        import jax
        import jax.numpy as jnp
        _gk = jax.random.key(seed)
        x = -0.0003713 + 1 * jax.random.normal(jax.random.fold_in(_gk, 1), (6250, 256), jnp.float32)
        src = jax.random.randint(jax.random.fold_in(_gk, 2), (200000,), 0, 6250, jnp.int32)
        dst = jnp.minimum((6250 * jax.random.uniform(jax.random.fold_in(_gk, 3), (200000,)) ** 2.0).astype(jnp.int32), 49999)
        _o = jnp.argsort(dst, stable=True)
        src = src[_o]
        dst = dst[_o]
        edge_attr_64 = 0.000151818 + 1.00006 * jax.random.normal(jax.random.fold_in(_gk, 11), (200000, 64), jnp.float32)
        edge_weight = jax.random.uniform(jax.random.fold_in(_gk, 13), (200000,), jnp.float32, 0.0, 4.99999)
        return (x, src, dst, edge_attr_64, edge_weight)
    x, src, dst, edge_attr_64, edge_weight = _rec_inputs()

    def _L0_gnn_setup():
        import jax, jax.numpy as jnp
        import numpy as np
        N, IN_CH, HEADS, OUT_CH, E = (6250, 256, 4, 64, 100000)
        key = jax.random.key(seed)
        k1, k2, k3, k4, k5 = jax.random.split(key, 5)
        x = jax.random.normal(k1, (N, IN_CH), dtype=jnp.float32)
        edge_index = jax.random.randint(k2, (2, E), 0, N, dtype=jnp.int64)
        bw = float(np.sqrt(6.0 / (IN_CH + HEADS * OUT_CH)))
        ba = float(np.sqrt(6.0 / (HEADS + OUT_CH)))
        weight = jax.random.uniform(k3, (IN_CH, HEADS * OUT_CH), jnp.float32, -bw, bw)
        attn_l = jax.random.uniform(k4, (HEADS, OUT_CH), jnp.float32, -ba, ba)
        attn_r = jax.random.uniform(k5, (HEADS, OUT_CH), jnp.float32, -ba, ba)
        return {'x': x, 'edge_index': edge_index, 'weight': weight, 'attn_l': attn_l, 'attn_r': attn_r}
    _L0_gnn_all = _L0_gnn_setup()
    _L0_gnn_in = {k: v for k, v in _L0_gnn_all.items() if k in ('weight', 'attn_l', 'attn_r')}
    del _L0_gnn_all

    def _L1_gnn_setup():
        import jax, jax.numpy as jnp
        import numpy as np
        H = 256
        R = 64
        N = 2500
        E = 40000
        CUTOFF_LO = 0.0
        CUTOFF_UP = 5.0
        LN_EPS = 1e-05

        def _layernorm(x, g, b):
            mu = jnp.mean(x, axis=-1, keepdims=True)
            var = jnp.var(x, axis=-1, keepdims=True)
            return (x - mu) * jax.lax.rsqrt(var + LN_EPS) * g + b

        def _cosine_cutoff(r):
            c = 0.5 * (jnp.cos(r * (jnp.pi / CUTOFF_UP)) + 1.0)
            return c * (r < CUTOFF_UP).astype(r.dtype)
        key = jax.random.key(seed)
        ks = jax.random.split(key, 16)

        def xavier(k, shape):
            fan_in, fan_out = (shape[1], shape[0])
            lim = np.sqrt(6.0 / (fan_in + fan_out))
            return jax.random.uniform(k, shape, jnp.float32, -lim, lim)
        x = jax.random.normal(ks[0], (N, H), jnp.float32)
        edge_index = jax.random.randint(ks[1], (2, E), 0, N, jnp.int64)
        edge_weight = jax.random.uniform(ks[2], (E,), jnp.float32, 0.0, CUTOFF_UP)
        edge_attr = jax.random.normal(ks[3], (E, R), jnp.float32)
        return {'x': x, 'edge_index': edge_index, 'edge_weight': edge_weight, 'edge_attr': edge_attr, 'ln_g': jnp.ones((H,), jnp.float32), 'ln_b': jnp.zeros((H,), jnp.float32), 'Wq': xavier(ks[4], (H, H)), 'bq': jnp.zeros((H,), jnp.float32), 'Wk': xavier(ks[5], (H, H)), 'bk': jnp.zeros((H,), jnp.float32), 'Wv': xavier(ks[6], (H, H)), 'bv': jnp.zeros((H,), jnp.float32), 'Wo': xavier(ks[7], (H, H)), 'bo': jnp.zeros((H,), jnp.float32), 'Wdk': xavier(ks[8], (H, R)), 'bdk': jnp.zeros((H,), jnp.float32), 'Wdv': xavier(ks[9], (H, R)), 'bdv': jnp.zeros((H,), jnp.float32)}
    _L1_gnn_all = _L1_gnn_setup()
    _L1_gnn_in = {k: v for k, v in _L1_gnn_all.items() if k in ('ln_g', 'ln_b', 'Wq', 'bq', 'Wk', 'bk', 'Wv', 'bv', 'Wo', 'bo', 'Wdk', 'bdk', 'Wdv', 'bdv')}
    del _L1_gnn_all
    return {'x': x, 'src': src, 'dst': dst, 'edge_attr_64': edge_attr_64, 'edge_weight': edge_weight, 'L0_gnn_weight': _L0_gnn_in['weight'], 'L0_gnn_attn_l': _L0_gnn_in['attn_l'], 'L0_gnn_attn_r': _L0_gnn_in['attn_r'], 'L1_gnn_ln_g': _L1_gnn_in['ln_g'], 'L1_gnn_ln_b': _L1_gnn_in['ln_b'], 'L1_gnn_Wq': _L1_gnn_in['Wq'], 'L1_gnn_bq': _L1_gnn_in['bq'], 'L1_gnn_Wk': _L1_gnn_in['Wk'], 'L1_gnn_bk': _L1_gnn_in['bk'], 'L1_gnn_Wv': _L1_gnn_in['Wv'], 'L1_gnn_bv': _L1_gnn_in['bv'], 'L1_gnn_Wo': _L1_gnn_in['Wo'], 'L1_gnn_bo': _L1_gnn_in['bo'], 'L1_gnn_Wdk': _L1_gnn_in['Wdk'], 'L1_gnn_bdk': _L1_gnn_in['bdk'], 'L1_gnn_Wdv': _L1_gnn_in['Wdv'], 'L1_gnn_bdv': _L1_gnn_in['bdv']}

def reference(x, src, dst, edge_attr_64, edge_weight, L0_gnn_weight, L0_gnn_attn_l, L0_gnn_attn_r, L1_gnn_ln_g, L1_gnn_ln_b, L1_gnn_Wq, L1_gnn_bq, L1_gnn_Wk, L1_gnn_bk, L1_gnn_Wv, L1_gnn_bv, L1_gnn_Wo, L1_gnn_bo, L1_gnn_Wdk, L1_gnn_bdk, L1_gnn_Wdv, L1_gnn_bdv):
    import jax
    import jax.numpy as jnp

    def _L0_gnn_ref(x, edge_index, weight, attn_l, attn_r):
        import jax, jax.numpy as jnp
        import numpy as np
        N, IN_CH, HEADS, OUT_CH, E = (6250, 256, 4, 64, 100000)
        heads, out_ch = attn_l.shape
        n = x.shape[0]
        xt = jnp.matmul(x, weight).reshape(-1, heads, out_ch)
        row, col = (edge_index[0], edge_index[1])
        alpha_l = jnp.einsum('ehd,hd->eh', xt[row], attn_l)
        alpha_r = jnp.einsum('ehd,hd->eh', xt[col], attn_r)
        alpha = jax.nn.softmax(jax.nn.leaky_relu(alpha_l + alpha_r, 0.01), axis=1)
        tmp = jnp.einsum('nh,nhd->nd', alpha[:n], xt[col[:n]])
        out = jnp.broadcast_to(tmp[:, None, :], (n, heads, out_ch))
        return out.reshape(n, heads * out_ch)

    def _L1_gnn_ref(x, edge_index, edge_weight, edge_attr, ln_g, ln_b, Wq, bq, Wk, bk, Wv, bv, Wo, bo, Wdk, bdk, Wdv, bdv):
        import jax, jax.numpy as jnp
        import numpy as np
        H = 256
        R = 64
        N = 2500
        E = 40000
        CUTOFF_LO = 0.0
        CUTOFF_UP = 5.0
        LN_EPS = 1e-05

        def _layernorm(x, g, b):
            mu = jnp.mean(x, axis=-1, keepdims=True)
            var = jnp.var(x, axis=-1, keepdims=True)
            return (x - mu) * jax.lax.rsqrt(var + LN_EPS) * g + b

        def _cosine_cutoff(r):
            c = 0.5 * (jnp.cos(r * (jnp.pi / CUTOFF_UP)) + 1.0)
            return c * (r < CUTOFF_UP).astype(r.dtype)
        src = edge_index[0]
        dst = edge_index[1]
        x_norm = _layernorm(x, ln_g, ln_b)
        q = x_norm @ Wq.T + bq
        k = x_norm @ Wk.T + bk
        v = x_norm @ Wv.T + bv
        dk = jax.nn.silu(edge_attr @ Wdk.T + bdk)
        dv = jax.nn.silu(edge_attr @ Wdv.T + bdv)
        q_i = q[dst]
        k_j = k[src]
        v_j = v[src]
        attn = jnp.sum(q_i * k_j * dk, axis=1)
        attn = jax.nn.silu(attn) * _cosine_cutoff(edge_weight)
        msg = v_j * dv * attn[:, None]
        agg = jax.ops.segment_sum(msg, dst, num_segments=x.shape[0])
        out = agg @ Wo.T + bo
        return x + out
    edge_index = jnp.stack([src, dst])
    x = _layernorm(x + _L0_gnn_ref(x, edge_index, L0_gnn_weight, L0_gnn_attn_l, L0_gnn_attn_r), axis=-1)
    x = _layernorm(x + _L1_gnn_ref(x, edge_index, edge_weight, edge_attr_64, L1_gnn_ln_g, L1_gnn_ln_b, L1_gnn_Wq, L1_gnn_bq, L1_gnn_Wk, L1_gnn_bk, L1_gnn_Wv, L1_gnn_bv, L1_gnn_Wo, L1_gnn_bo, L1_gnn_Wdk, L1_gnn_bdk, L1_gnn_Wdv, L1_gnn_bdv), axis=-1)
    return x

_drawn_inputs = setup_inputs


def setup_inputs(seed=0):
    import zlib

    import numpy as np

    out = dict(_drawn_inputs(seed))
    spreads = {'L1_gnn_ln_g': (1.0, 0.2),
     'L1_gnn_ln_b': (0.0, 0.1),
     'L1_gnn_bq': (0.0, 0.1),
     'L1_gnn_bk': (0.0, 0.1),
     'L1_gnn_bv': (0.0, 0.1),
     'L1_gnn_bo': (0.0, 0.396),
     'L1_gnn_bdk': (0.0, 0.1),
     'L1_gnn_bdv': (0.0, 0.1)}
    factors = {}
    for name, (base, spread) in spreads.items():
        noise = np.random.default_rng([zlib.crc32(name.encode()), seed]).standard_normal(out[name].shape)
        drawn = base * np.exp(spread * noise) if base else spread * noise
        out[name] = jnp.asarray(drawn.astype(out[name].dtype))
    for name, factor in factors.items():
        out[name] = (out[name] * factor).astype(out[name].dtype)
    return out
```

```python
import math
from contextlib import ExitStack

import concourse.bass as bass
from concourse import mybir

P = 128
F32 = mybir.dt.float32
F32R = mybir.dt.float32r
BF16 = mybir.dt.bfloat16
I32 = mybir.dt.int32
U32 = mybir.dt.uint32
ALU = mybir.AluOpType
ACT = mybir.ActivationFunctionType
AX = mybir.AxisListType
EPS = 1e-5
SLOPE = 0.01
CUTOFF = 5.0

H = 256
HEADS = 4
DH = H // HEADS
R = 64
LOT = 10
GROUP = 4
SPAN = P * GROUP
TURN_TILES = 8
BLOCK_TURNS = 2
BLOCK_TILES = TURN_TILES * BLOCK_TURNS
BLOCK = P * BLOCK_TILES


class Turns:
    KINDS = {"now": (1, 1), "next": (2, 1), "after": (3, 1),
             "now16": (16, 16), "next16": (32, 16),
             "tiles": (LOT, LOT), "tiles_before": (0, LOT)}

    def __init__(self, eng, name, kinds):
        self.eng, self.kinds = eng, kinds.split()
        self.now, self.next, self.after, self.now16, self.next16, self.tiles, self.tiles_before = (
            eng.alloc_register(f"{name}_{x}") if x in self.kinds else None
            for x in ("now", "next", "after", "now16", "next16", "tiles", "tiles_before"))
        for register, kind in self.registers():
            eng.reg_mov(register, self.KINDS[kind][0])
        if self.tiles or self.tiles_before:
            self.reached = eng.alloc_register(f"{name}_reached")

    def registers(self):
        every = {"now": self.now, "next": self.next, "after": self.after, "now16": self.now16, "next16": self.next16,
                 "tiles": self.tiles, "tiles_before": self.tiles_before}
        return [(every[kind], kind) for kind in self.kinds]

    def tile(self, j):
        return self.eng.snap(self.tiles, min_val=LOT) + (j + 1)

    def tile_before(self, j):
        return self.eng.snap(self.tiles_before, min_val=0) + (j + 1)

    def reach(self, j):
        self.eng.reg_add(self.reached, self.tiles, j + 1)
        return self.reached

    def reach_before(self, j):
        self.eng.reg_add(self.reached, self.tiles_before, j + 1)
        return self.reached

    def step(self):
        for register, kind in self.registers():
            self.eng.reg_add(register, register, self.KINDS[kind][1])


def gnn_kernel(nc, x, src_tiles, dst_tiles, edge_weight_tiles, src_first, dst_first, edge_attr_t,
               weight, attn_l, attn_r, ln_g, ln_b, wqkv_t, bqkv, wo_t, bo, wd_t, bd, out):
    N = x.shape[0]
    E = edge_attr_t.shape[1]
    BLOCKS = -(-E // BLOCK)
    TILES = -(-N // (P * LOT)) * LOT
    NP = TILES * P
    assert NP >= N + P, "a window that starts at the last node stays in the tables"
    LOTS = TILES // LOT
    FULL, REST = N // P, N % P
    TAB = H + 2 * HEADS
    MASKED = BLOCKS * BLOCK - E

    xt_tab = nc.dram_tensor("xt_tab", (NP, TAB), F32, kind="Internal").ap()
    q_tab = nc.dram_tensor("q_tab", (NP, 2 * H), F32, kind="Internal").ap()
    kv_tab = nc.dram_tensor("kv_tab", (NP, 2 * H), F32, kind="Internal").ap()
    sum_tab = nc.dram_tensor("sum_tab", (NP, H), F32, kind="Internal").ap()

    with ExitStack() as top:
        def keep(name, shape, dt):
            return top.enter_context(nc.sbuf_tensor(name, shape, dt))

        x_sb = keep("x_sb", [P, TILES, H], F32)
        ident = keep("ident", [P, P], F32)
        ident_bf = keep("ident_bf", [P, P], BF16)
        iota = keep("iota", [P, P], F32)
        steps = keep("steps", [P, 64], F32)
        wqkv = keep("wqkv", [P, 2, 3 * H], F32)
        bias_qkv = keep("bias_qkv", [P, 3 * H], F32)
        wo = keep("wo", [P, 2, H], F32)
        bo_rep = keep("bo_rep", [P, H], F32)
        src_idx = keep("src_idx", [P, BLOCKS * BLOCK_TILES], I32)
        dst_f = keep("dst_f", [P, BLOCKS * BLOCK_TILES], F32)
        cut = keep("cut", [P, BLOCKS * BLOCK_TILES], F32)
        first_idx = keep("first_idx", [P, 2, TILES], I32)
        window_f = keep("window_f", [P, BLOCKS], F32)
        walk = keep("walk", [P, 4, BLOCKS], I32)
        wd_hi_lo = keep("wd_hi_lo", [P, 2 * H], F32R)
        wd_bias = keep("wd_bias", [P, 2 * H], F32R)

        with nc.cleanup_on_exit(), ExitStack() as ctx:
            def sb(name, shape, dt):
                return ctx.enter_context(nc.sbuf_tensor(name, shape, dt))

            def psum(name, shape, dt):
                return ctx.enter_context(nc.psum_tensor(name, shape, dt))

            def sem(name):
                return nc.alloc_semaphore(name=name)

            w_ext = sb("w_ext", [P, 2, TAB], F32)
            attn = sb("attn", [P, 2, H], F32)
            w_attn = sb("w_attn", [P, 2, 2, H], F32)
            x_in = sb("x_in", [P, LOT, H], F32)
            x_t = sb("x_t", [P, 2, 2 * P], F32)
            xt_out = sb("xt_out", [P, LOT, TAB], F32)
            zeros = sb("zeros", [P, H], F32)
            ln_cols = sb("ln_cols", [P, 2, 2], F32)
            b_wide = sb("b_wide", [P, 2, P], F32)
            bqkv_rep = sb("bqkv_rep", [P, 3 * H], F32)
            dst_i = sb("dst_i", [P, BLOCKS * BLOCK_TILES], I32)
            dist = sb("dist", [P, BLOCKS * BLOCK_TILES], F32)
            turns_i = sb("turns_i", [P, BLOCKS * BLOCK_TILES], I32)
            wrapped = sb("wrapped", [P, BLOCKS * BLOCK_TILES], F32)
            phase = sb("phase", [P, BLOCKS * BLOCK_TILES], F32)
            ends = sb("ends", [P, 2, BLOCKS], F32)
            all_ends = sb("all_ends", [P, 2, BLOCKS], F32)
            spread = sb("spread", [P, BLOCKS], F32)
            spread_i = sb("spread_i", [P, BLOCKS], I32)
            iota_i = sb("iota_i", [P, P], I32)
            steps_i = sb("steps_i", [P, 64], I32)
            half_pi = sb("half_pi", [P, 1], F32)
            wd_raw = sb("wd_raw", [P, 2 * H], F32)
            bd_raw = sb("bd_raw", [P, 2 * H], F32)

            turned_ps = psum("turned_ps", [P, 2, 512], F32)
            xt_ps = psum("xt_ps", [P, 2, 512], F32)
            bias_ps = [psum(f"bias_ps{s}", [P, 512], F32) for s in range(2)]

            x_landed, pad_zero = sem("x_landed"), sem("pad_zero")
            w_landed, ln_landed, idx_landed, bias_landed, wd_landed, small_landed = (
                sem(n) for n in ("w_landed", "ln_landed", "idx_landed", "bias_landed", "wd_landed", "small_landed"))
            ident_zero, ident_ready, iota_ready = (sem(n) for n in ("ident_zero", "ident_ready", "iota_ready"))
            zero_ready, sums_zeroed = sem("zero_ready"), sem("sums_zeroed")
            w_ready = sem("w_ready")
            dve_step, ends_ready, all_ready, cut_step = (
                sem(n) for n in ("dve_step", "ends_ready", "all_ready", "cut_step"))
            b_ready, bias_done, bias_used, wd_rounded = (
                sem(n) for n in ("b_ready", "bias_done", "bias_used", "wd_rounded"))
            go = sem("go")
            angle_ready, sine_ready, bd_zero = sem("angle_ready"), sem("sine_ready"), sem("bd_zero")
            landed, stored = ([sem(f"{n}{j}") for j in range(LOT)] for n in ("landed", "stored"))
            turned, turned_copied, projected, projected_copied, out_free = (
                sem(n) for n in ("turned", "turned_copied", "projected", "projected_copied", "out_free"))

            with nc.Block() as block:
                @block.sync
                def _(sp):
                    sp.dma_start(w_ext[:, :, 0:H], weight.rearrange("(k p) n -> p k n", p=P)).then_inc(w_landed, 16)
                    sp.dma_start(attn[:, 0, :], attn_l.rearrange("h d -> (h d)").partition_broadcast(P)).then_inc(w_landed, 16)
                    sp.dma_start(attn[:, 1, :], attn_r.rearrange("h d -> (h d)").partition_broadcast(P)).then_inc(w_landed, 16)
                    sp.wait_ge(zero_ready, 1)
                    turn = Turns(sp, "sp_project", "now16 tiles")
                    sp.sem_inc(out_free, LOT)

                    def release(j):
                        sp.wait_ge(stored[j], turn.now16)
                        sp.sem_inc(out_free, 1)

                    with sp.Fori(0, LOTS) as lot:
                        sp.dma_start(sum_tab[bass.ds(lot * (LOT * P), LOT * P), :].rearrange("(i p) c -> p i c", p=P),
                                     zeros[:].unsqueeze(1).broadcast_to([P, LOT, H])).then_inc(sums_zeroed, 16)
                        for j in range(LOT):
                            reached = turn.reach(j)
                            sp.wait_ge(go, 1)
                            sp.wait_ge(projected_copied, reached)
                            sp.dma_start(xt_tab[bass.ds(lot * (LOT * P) + j * P, P), :], xt_out[:, j, :]).then_inc(stored[j], 16)
                            if j >= 4:
                                release(j - 4)
                        for j in range(LOT - 4, LOT):
                            release(j)
                        turn.step()
                    sp.wait_ge(sums_zeroed, 16 * LOTS)

                @block.gpsimd
                def _(pool):
                    turn = Turns(pool, "pool_project", "tiles_before")
                    pool.sem_inc(go, 1)
                    for j in range(LOT):
                        pool.dma_start(x_in[:, j, :], x[j * P:(j + 1) * P, :]).then_inc(landed[j], 16)
                    turn.step()
                    nc.gpsimd.memset(ident[:], 0.0).then_inc(ident_zero, 1)
                    nc.gpsimd.memset(ident_bf[:], 0.0).then_inc(ident_zero, 1)
                    pool.wait_ge(ident_zero, 2)
                    for t in (ident, ident_bf):
                        nc.gpsimd.affine_select(out=t[:], in_=t[:], compare_op=ALU.not_equal, fill=1.0,
                                                base=0, pattern=[[-1, P]], channel_multiplier=1).then_inc(ident_ready, 1)
                    nc.gpsimd.iota(iota_i[:], pattern=[[1, P]], base=0, channel_multiplier=0).then_inc(iota_ready, 1)
                    nc.gpsimd.iota(steps_i[:], pattern=[[P, 64]], base=0, channel_multiplier=0).then_inc(iota_ready, 1)
                    nc.gpsimd.iota(walk[:, 2, :], pattern=[[BLOCK, BLOCKS]], base=0, channel_multiplier=0).then_inc(iota_ready, 1)
                    nc.gpsimd.memset(x_sb[:, FULL:TILES, :], 0.0).then_inc(pad_zero, 1)

                    pool.wait_ge(ends_ready, 2)
                    nc.gpsimd.partition_all_reduce(all_ends[:].rearrange("p a b -> p (a b)"), ends[:].rearrange("p a b -> p (a b)"),
                                                   P, bass.bass_isa.ReduceOp.max).then_inc(all_ready, 1)

                    def load(row, j, rows):
                        reached = turn.reach_before(j)
                        pool.wait_ge(go, 1)
                        pool.wait_ge(turned, reached)
                        pool.dma_start(x_in[0:rows, j, :], x[row, :]).then_inc(landed[j], 16)

                    if LOTS > 2:
                        with pool.Fori(1, LOTS - 1) as lot:
                            for j in range(LOT):
                                load(bass.ds(lot * (LOT * P) + j * P, P), j, P)
                            turn.step()
                    for j in range(LOT):
                        first = ((LOTS - 1) * LOT + j) * P
                        if first < N:
                            rows = min(P, N - first)
                            load(slice(first, first + rows), j, rows)

                @block.scalar
                def _(act):
                    act.dma_start(dst_i[:], dst_tiles).then_inc(idx_landed, 16)
                    act.dma_start(dist[:], edge_weight_tiles).then_inc(idx_landed, 16)
                    act.dma_start(ln_cols[:, 0, :], ln_g).then_inc(ln_landed, 16)
                    act.dma_start(ln_cols[:, 1, :], ln_b).then_inc(ln_landed, 16)
                    act.dma_start(wqkv[:], wqkv_t.rearrange("(k p) n -> p k n", p=P)).then_inc(bias_landed, 16)
                    act.dma_start(bqkv_rep[:], bqkv.partition_broadcast(P)).then_inc(bias_landed, 16)
                    act.dma_start(src_idx[:], src_tiles).then_inc(small_landed, 16)
                    act.dma_start(first_idx[:, 0, :], src_first).then_inc(small_landed, 16)
                    act.dma_start(first_idx[:, 1, :], dst_first).then_inc(small_landed, 16)
                    act.dma_start(wo[:], wo_t.rearrange("(k p) n -> p k n", p=P)).then_inc(small_landed, 16)
                    act.dma_start(bo_rep[:], bo.partition_broadcast(P)).then_inc(small_landed, 16)
                    act.dma_start(wd_raw[0:R, :], wd_t).then_inc(wd_landed, 16)
                    act.dma_start(wd_raw[R:P, :], wd_t).then_inc(wd_landed, 16)
                    act.wait_ge(bd_zero, 1)
                    act.dma_start(bd_raw[64:65, :], bd.unsqueeze(0)).then_inc(wd_landed, 16)
                    act.dma_start(bd_raw[96:97, :], bd.unsqueeze(0)).then_inc(wd_landed, 16)
                    act.dma_start(x_sb[:, 0:FULL, :], x[0:FULL * P, :].rearrange("(i p) c -> p i c", p=P)).then_inc(x_landed, 16)
                    act.wait_ge(pad_zero, 1)
                    act.dma_start(x_sb[0:REST, FULL, :], x[FULL * P:N, :]).then_inc(x_landed, 16)
                    turn = Turns(act, "act_project", "tiles tiles_before")
                    act.sem_inc(turned_copied, LOT)
                    nc.scalar.preload_act_table(ACT.Sin)
                    with act.Fori(0, LOTS):
                        for j in range(LOT):
                            act.wait_ge(turned, turn.tile(j))
                            wait_slot(act, projected, j, turn)
                            nc.scalar.copy(x_t[:, j % 2, :], turned_ps[:, j % 2, 0:H]).then_inc(turned_copied, 1)
                        turn.step()
                    act.wait_ge(wd_landed, 64)
                    nc.scalar.copy(wd_hi_lo[:], wd_raw[:]).then_inc(wd_rounded, 1)
                    nc.scalar.copy(wd_bias[0:R, :], wd_raw[0:R, :]).then_inc(wd_rounded, 1)
                    nc.scalar.copy(wd_bias[R:P, :], bd_raw[R:P, :]).then_inc(wd_rounded, 1)
                    act.wait_ge(angle_ready, 1)
                    nc.scalar.activation(phase[:], wrapped[:], ACT.Sin, bias=half_pi[:], scale=-math.pi / CUTOFF).then_inc(sine_ready, 1)
                    act.wait_ge(x_landed, 32)
                    act.wait_ge(small_landed, 16 * 5)

                @block.tensor
                def _(pe):
                    pe.wait_ge(ident_ready, 2)
                    turn = Turns(pe, "pe_project", "now16 tiles tiles_before")
                    pe.sem_inc(turned, LOT)
                    pe.sem_inc(projected, LOT)

                    def turn_tile(j, lands):
                        if lands:
                            pe.wait_ge(landed[j], turn.now16)
                        wait_slot(pe, turned_copied, j, turn)
                        for k in range(2):
                            last = nc.tensor.transpose(turned_ps[:, j % 2, k * P:(k + 1) * P], x_in[:, j, k * P:(k + 1) * P], ident[:])
                        last.then_inc(turned, 1)

                    def lot_products(lands):
                        turn_tile(0, lands[0])
                        for j in range(LOT):
                            if j + 1 < LOT:
                                turn_tile(j + 1, lands[j + 1])
                            pe.wait_ge(turned_copied, turn.tile(j))
                            wait_slot(pe, projected_copied, j, turn)
                            for k in range(2):
                                last = nc.tensor.matmul(xt_ps[:, j % 2, 0:TAB], x_t[:, j % 2, k * P:(k + 1) * P], w_ext[:, k, :], start=(k == 0), stop=(k == 1))
                            last.then_inc(projected, 1)
                        turn.step()

                    pe.wait_ge(b_ready, 1)
                    pe.wait_ge(bias_landed, 32)
                    for part, (a, b) in enumerate(((0, 512), (512, 768))):
                        for k in range(2):
                            last = nc.tensor.matmul(bias_ps[part][:, 0:b - a], b_wide[:, k, :], wqkv[:, k, a:b], start=(k == 0), stop=(k == 1))
                        last.then_inc(bias_done, 1)
                    pe.wait_ge(w_ready, 1)
                    with pe.Fori(0, LOTS - 1):
                        lot_products([True] * LOT)
                    lot_products([((LOTS - 1) * LOT + j) * P < N for j in range(LOT)])

                @block.vector
                def _(dve):
                    count = [0]

                    def then(ins):
                        count[0] += 1
                        ins.then_inc(dve_step, 1)
                        dve.wait_ge(dve_step, count[0])

                    nc.vector.memset(zeros[:], 0.0).then_inc(zero_ready, 1)
                    nc.vector.memset(half_pi[:], math.pi / 2)
                    nc.vector.memset(bd_raw[:], 0.0).then_inc(bd_zero, 1)
                    dve.wait_ge(w_landed, 48)
                    for a in range(2):
                        for k in range(2):
                            last = nc.vector.tensor_tensor(w_attn[:, a, k, :], w_ext[:, k, 0:H], attn[:, a, :], ALU.mult)
                    then(last)
                    for a in range(2):
                        for k in range(2):
                            last = nc.vector.tensor_reduce(w_ext[:, k, H + a * HEADS:H + (a + 1) * HEADS],
                                                           w_attn[:, a, k, :].rearrange("p (h d) -> p h d", h=HEADS), AX.X, ALU.add)
                    last.then_inc(w_ready, 1)
                    dve.wait_ge(ln_landed, 32)
                    nc.vector.tensor_copy(b_wide[:], ln_cols[:, 1, :].unsqueeze(2).broadcast_to([P, 2, P])).then_inc(b_ready, 1)
                    dve.wait_ge(idx_landed, 32)
                    then(nc.vector.tensor_copy(dst_f[:], dst_i[:]))
                    by_block = dst_f[:].rearrange("p (b j) -> p b j", j=BLOCK_TILES)
                    nc.vector.tensor_reduce(ends[:, 1, :], by_block, AX.X, ALU.max).then_inc(ends_ready, 1)
                    then(nc.vector.tensor_reduce(ends[:, 0, :], by_block, AX.X, ALU.min))
                    nc.vector.tensor_scalar(ends[:, 0, :], ends[:, 0, :], -1.0, None, ALU.mult).then_inc(ends_ready, 1)
                    dve.wait_ge(ends_ready, 2)
                    tail = (BLOCKS - 1) * BLOCK_TILES
                    for g in range(BLOCK // SPAN):
                        rows = min(max(MASKED - g * SPAN, 0), SPAN) // GROUP
                        if rows:
                            nc.vector.memset(dst_f[0:rows, tail + g * GROUP:tail + (g + 1) * GROUP], -1.0)
                    then(nc.vector.tensor_scalar(cut[:], dist[:], CUTOFF, None, ALU.is_lt))
                    then(nc.vector.tensor_scalar(dist[:], dist[:], CUTOFF, None, ALU.min))
                    then(nc.vector.tensor_scalar(turns_i[:], dist[:], 0.5 / CUTOFF, None, ALU.mult))
                    then(nc.vector.tensor_copy(wrapped[:], turns_i[:]))
                    then(nc.vector.scalar_tensor_tensor(out=wrapped[:], in0=wrapped[:], scalar=-2 * CUTOFF, in1=dist[:], op0=ALU.mult, op1=ALU.add))
                    then(nc.vector.scalar_tensor_tensor(out=wrapped[:], in0=wrapped[:], scalar=-1.0, in1=wrapped[:], op0=ALU.mult, op1=ALU.max))
                    then(nc.vector.tensor_scalar(wrapped[:], wrapped[:], -CUTOFF, None, ALU.add))
                    nc.vector.scalar_tensor_tensor(out=wrapped[:], in0=wrapped[:], scalar=-1.0, in1=wrapped[:], op0=ALU.mult, op1=ALU.max).then_inc(angle_ready, 1)
                    dve.wait_ge(bias_done, 2)
                    nc.vector.tensor_tensor(bias_qkv[:, 0:512], bias_ps[0][:], bqkv_rep[:, 0:512], ALU.add)
                    nc.vector.tensor_tensor(bias_qkv[:, 512:768], bias_ps[1][:, 0:256], bqkv_rep[:, 512:768], ALU.add)
                    for k in range(2):
                        nc.vector.tensor_scalar(wqkv[:, k, :], wqkv[:, k, :], ln_cols[:, 0, k:k + 1], None, ALU.mult)
                    dve.wait_ge(all_ready, 1)
                    nc.vector.tensor_scalar(window_f[:], all_ends[:, 0, :], -1.0, None, ALU.mult)
                    then(nc.vector.tensor_tensor(spread[:], all_ends[:, 1, :], all_ends[:, 0, :], ALU.add))
                    nc.vector.tensor_copy(walk[:, 1, :], window_f[:])
                    then(nc.vector.tensor_copy(spread_i[:], spread[:]))
                    then(nc.vector.tensor_single_scalar(spread_i[:], spread_i[:], 7, ALU.arith_shift_right))
                    nc.vector.tensor_scalar(walk[:, 0, :], spread_i[:], 1, None, ALU.add)
                    dve.wait_ge(iota_ready, 3)
                    nc.vector.tensor_copy(steps[:], steps_i[:])
                    nc.vector.tensor_scalar(walk[:, 2, :], walk[:, 2, :], E - BLOCK, None, ALU.min)
                    nc.vector.tensor_copy(iota[:], iota_i[:])
                    turn = Turns(dve, "dve_project", "tiles tiles_before")
                    dve.sem_inc(projected_copied, LOT)
                    with dve.Fori(0, LOTS):
                        for j in range(LOT):
                            dve.wait_ge(projected, turn.tile(j))
                            dve.wait_ge(out_free, turn.tile_before(j))
                            nc.vector.tensor_copy(xt_out[:, j, :], xt_ps[:, j % 2, 0:TAB]).then_inc(projected_copied, 1)
                        turn.step()
                    dve.wait_ge(wd_rounded, 3)
                    nc.vector.tensor_tensor(wd_hi_lo[R:P, :], wd_raw[R:P, :], wd_hi_lo[R:P, :], ALU.subtract)
                    nc.vector.tensor_tensor(wd_bias[96:97, :], bd_raw[96:97, :], wd_bias[96:97, :], ALU.subtract)
                    dve.wait_ge(sine_ready, 1)
                    then(nc.vector.tensor_scalar(phase[:], phase[:], -0.5, 0.5, ALU.mult, ALU.add))
                    nc.vector.tensor_tensor(cut[:], cut[:], phase[:], ALU.mult)

        layer0(nc, dict(
            x_sb=x_sb, ident=ident, wqkv=wqkv, bias_qkv=bias_qkv, first_idx=first_idx,
            xt_tab=xt_tab, q_tab=q_tab, kv_tab=kv_tab, TILES=TILES, LOTS=LOTS, TAB=TAB))
        edge_stage(nc, dict(
            ident_bf=ident_bf, iota=iota, steps=steps, src_idx=src_idx, dst_f=dst_f, cut=cut, window_f=window_f, walk=walk,
            wd_hi_lo=wd_hi_lo, wd_bias=wd_bias, q_tab=q_tab, kv_tab=kv_tab, sum_tab=sum_tab, edge_attr_t=edge_attr_t,
            NP=NP, N=N, E=E, BLOCKS=BLOCKS))
        output_stage(nc, dict(
            x_sb=x_sb, ident=ident, wo=wo, bo_rep=bo_rep, sum_tab=sum_tab, out=out, TILES=TILES, LOTS=LOTS, N=N))


def wait_slot(eng, group, j, turn):
    if j >= 2:
        eng.wait_ge(group, turn.tile(j - 2))
    else:
        eng.wait_ge(group, turn.tile_before(LOT - 2 + j))


class Scope:

    def __init__(self, nc, ctx, prefix):
        self.nc, self.ctx, self.prefix = nc, ctx, prefix

    def sb(self, name, shape, dt):
        return self.ctx.enter_context(self.nc.sbuf_tensor(self.prefix + name, shape, dt))

    def psum(self, name, shape, dt):
        return self.ctx.enter_context(self.nc.psum_tensor(self.prefix + name, shape, dt))

    def sem(self, name):
        return self.nc.alloc_semaphore(name=self.prefix + name)

    def sems(self, name, n):
        return [self.sem(f"{name}{j}") for j in range(n)]


def layer0(nc, shared):
    x_sb, ident, wqkv, bias_qkv, first_idx = (shared[n] for n in ("x_sb", "ident", "wqkv", "bias_qkv", "first_idx"))
    xt_tab, q_tab, kv_tab, TILES, LOTS, TAB = (shared[n] for n in ("xt_tab", "q_tab", "kv_tab", "TILES", "LOTS", "TAB"))
    with nc.cleanup_on_exit(), ExitStack() as ctx:
        scope = Scope(nc, ctx, "l0_")
        sb, psum, sem, sems = scope.sb, scope.psum, scope.sem, scope.sems

        idx = sb("idx", [P, 2, LOT], I32)
        by_src = sb("by_src", [P, LOT, TAB], F32)
        by_dst = sb("by_dst", [P, LOT, TAB], F32)
        score = sb("score", [P, LOT, HEADS], F32)
        leaky = sb("leaky", [P, LOT, HEADS], F32)
        top_score = sb("top_score", [P, LOT], F32)
        prob = sb("prob", [P, LOT, HEADS], F32)
        total = sb("total", [P, LOT], F32)
        weighed = sb("weighed", [P, 3, H], F32)
        mixed = sb("mixed", [P, 3, DH], F32)
        stats = sb("stats", [P, LOT, 6], F32)
        mean_var = sb("mean_var", [P, LOT, 2], F32)
        inverse = sb("inverse", [P, LOT], F32)
        rstd = sb("rstd", [P, LOT], F32)
        shift = sb("shift", [P, LOT], F32)
        summed = sb("summed", [P, LOT, H], F32)
        normed = sb("normed", [P, LOT, H], F32)
        normed_t = sb("normed_t", [P, 2, 2 * P], F32)
        q_full = sb("q_full", [P, LOT, H], F32)
        q_out = sb("q_out", [P, LOT, 2 * H], F32R)
        kv_out = sb("kv_out", [P, LOT, 2 * H], F32)

        turned_ps = psum("turned_ps", [P, 2, 512], F32)
        q_ps = psum("q_ps", [P, 2, 512], F32)
        kv_ps = psum("kv_ps", [P, 2, 2 * H], F32)

        src_landed, dst_landed = sems("src_landed", LOT), sems("dst_landed", LOT)
        idx_ready = sems("idx_ready", 2)
        scored, leaked, topped, centred, exped, totalled, inverted, alpha_ready = (
            sem(n) for n in ("scored", "leaked", "topped", "centred", "exped", "totalled", "inverted", "alpha_ready"))
        weighed_ready, mixed_ready, sum_ready, stat_ready, x1_ready, stat2_ready, normed_ready = (
            sem(n) for n in ("weighed", "mixed", "sum", "stat", "x1", "stat2", "normed_ready"))
        var_ready, inverse_ready, rstd_ready, shift_ready, var2_ready, inverse2_ready, rstd2_ready, shift2_ready = (
            sem(n) for n in ("var_ready", "inverse_ready", "rstd_ready", "shift_ready", "var2_ready", "inverse2_ready", "rstd2_ready", "shift2_ready"))
        padded, padded2 = sem("padded"), sem("padded2")
        turned, turned_copied, q_done, kv_done, q_copied, q_high, q_low, kv_copied, out_free = (
            sem(n) for n in ("turned", "turned_copied", "q_done", "kv_done", "q_copied", "q_high", "q_low", "kv_copied", "out_free"))
        stored, stored2 = sems("stored", LOT), sems("stored2", LOT)
        go = sem("go")

        with nc.Block() as block:
            @block.gpsimd
            def _(pool):
                turn = Turns(pool, "pool_l0", "now next tiles_before")
                pool.sem_inc(go, 1)
                for s in idx_ready:
                    pool.sem_inc(s, 1)

                def copy_indices(end, lot):
                    nc.gpsimd.tensor_copy(idx[:, end, :], first_idx[:, end, bass.ds(lot * LOT, LOT)]).then_inc(idx_ready[end], 1)
                    pool.wait_ge(go, 1)
                    pool.wait_ge(idx_ready[end], turn.next)

                with pool.Fori(0, LOTS) as lot:
                    pool.wait_ge(scored, turn.now)
                    copy_indices(0, lot)
                    for j in range(LOT):
                        pool.indirect_dma_start(by_src[:, j, :], None, xt_tab,
                                                bass.IndirectOffsetOnAxis(ap=idx[:, 0, j:j + 1], axis=0)).then_inc(src_landed[j], 16)
                    pool.wait_ge(weighed_ready, turn.tile_before(LOT - 1))
                    copy_indices(1, lot)
                    for j in range(LOT):
                        reached = turn.reach_before(j)
                        pool.wait_ge(go, 1)
                        pool.wait_ge(weighed_ready, reached)
                        pool.indirect_dma_start(by_dst[:, j, :], None, xt_tab,
                                                bass.IndirectOffsetOnAxis(ap=idx[:, 1, j:j + 1], axis=0)).then_inc(dst_landed[j], 16)
                    turn.step()

            @block.sync
            def _(sp):
                turn = Turns(sp, "sp_l0", "now16 tiles")
                sp.sem_inc(out_free, 2 * LOT)

                def release(j):
                    sp.wait_ge(stored[j], turn.now16)
                    sp.wait_ge(stored2[j], turn.now16)
                    sp.sem_inc(out_free, 1)

                with sp.Fori(0, LOTS) as lot:
                    for j in range(LOT):
                        reached = turn.reach(j)
                        sp.wait_ge(go, 1)
                        sp.wait_ge(q_low, reached)
                        sp.dma_start(q_tab[bass.ds(lot * (LOT * P) + j * P, P), :], q_out[:, j, :].bitcast(F32)).then_inc(stored[j], 16)
                        reached = turn.reach(j)
                        sp.wait_ge(go, 1)
                        sp.wait_ge(kv_copied, reached)
                        sp.dma_start(kv_tab[bass.ds(lot * (LOT * P) + j * P, P), :], kv_out[:, j, :]).then_inc(stored2[j], 16)
                        if j >= 4:
                            release(j - 4)
                    for j in range(LOT - 4, LOT):
                        release(j)
                    turn.step()

            @block.tensor
            def _(pe):
                turn = Turns(pe, "pe_l0", "tiles tiles_before")
                pe.sem_inc(turned, LOT)
                pe.sem_inc(q_done, LOT)
                pe.sem_inc(kv_done, 2 * LOT)
                with pe.Fori(0, LOTS) as lot:
                    def turn_tile(j):
                        pe.wait_ge(normed_ready, turn.tile(j))
                        wait_slot(pe, turned_copied, j, turn)
                        for k in range(2):
                            last = nc.tensor.transpose(turned_ps[:, j % 2, k * P:(k + 1) * P], normed[:, j, k * P:(k + 1) * P], ident[:])
                        last.then_inc(turned, 1)

                    turn_tile(0)
                    for j in range(LOT):
                        if j + 1 < LOT:
                            turn_tile(j + 1)
                        pe.wait_ge(turned_copied, turn.tile(j))
                        wait_slot(pe, q_copied, j, turn)
                        for k in range(2):
                            last = nc.tensor.matmul(q_ps[:, j % 2, 0:H], normed_t[:, j % 2, k * P:(k + 1) * P], wqkv[:, k, 0:H],
                                                    start=(k == 0), stop=(k == 1))
                        last.then_inc(q_done, 1)
                        wait_slot(pe, kv_copied, j, turn)
                        for k in range(2):
                            last = nc.tensor.matmul(kv_ps[:, j % 2, :], normed_t[:, j % 2, k * P:(k + 1) * P], wqkv[:, k, H:3 * H],
                                                    start=(k == 0), stop=(k == 1))
                        last.then_inc(kv_done, 1)
                    turn.step()

            @block.scalar
            def _(act):
                turn = Turns(act, "act_l0", "now next tiles tiles_before")
                for s in (exped, rstd_ready, rstd2_ready):
                    act.sem_inc(s, 1)
                for s in (turned_copied, x1_ready, normed_ready, q_high):
                    act.sem_inc(s, LOT)

                def copy_turned(j):
                    act.wait_ge(turned, turn.tile_before(j))
                    if j >= 2:
                        act.wait_ge(kv_done, turn.tile(j - 2))
                    else:
                        act.wait_ge(kv_done, turn.tile_before(LOT - 2 + j))
                    nc.scalar.copy(normed_t[:, j % 2, :], turned_ps[:, j % 2, 0:H]).then_inc(turned_copied, 1)

                def round_q(j):
                    act.wait_ge(q_copied, turn.tile_before(j))
                    nc.scalar.copy(q_out[:, j, 0:H], q_full[:, j, :]).then_inc(q_high, 1)

                def probabilities():
                    act.wait_ge(centred, turn.next)
                    act.wait_ge(alpha_ready, turn.now)
                    nc.scalar.activation(prob[:], score[:], ACT.Exp).then_inc(exped, 1)

                def root(inverses, scales):
                    act.wait_ge(inverses, turn.next)
                    nc.scalar.activation(rstd[:], inverse[:], ACT.Sqrt).then_inc(scales, 1)

                def first_norm(lot):
                    root(inverse_ready, rstd_ready)
                    act.wait_ge(shift_ready, turn.next)
                    for j in range(LOT):
                        nc.scalar.activation(x_sb[:, bass.ds(lot * LOT + j, 1), :].rearrange("p a c -> p (a c)"), summed[:, j, :], ACT.Identity,
                                             bias=shift[:, j:j + 1], scale=rstd[:, j:j + 1]).then_inc(x1_ready, 1)

                def second_norm(lot):
                    root(inverse2_ready, rstd2_ready)
                    act.wait_ge(shift2_ready, turn.next)
                    for j in range(LOT):
                        reached = turn.reach_before(j)
                        act.wait_ge(go, 1)
                        act.wait_ge(turned, reached)
                        nc.scalar.activation(normed[:, j, :],
                                             x_sb[:, bass.ds(lot * LOT + j, 1), :].rearrange("p a c -> p (a c)"), ACT.Identity,
                                             bias=shift[:, j:j + 1], scale=rstd[:, j:j + 1]).then_inc(normed_ready, 1)

                probabilities()
                first_norm(0)
                second_norm(0)
                turn.step()
                with act.Fori(1, LOTS) as lot:
                    probabilities()
                    for j in range(LOT - 1):
                        copy_turned(j)
                        if 1 <= j < LOT - 2:
                            round_q(j - 1)
                    first_norm(lot)
                    copy_turned(LOT - 1)
                    for j in range(LOT - 3, LOT):
                        round_q(j)
                    second_norm(lot)
                    turn.step()
                for j in range(LOT + 1):
                    if j < LOT:
                        copy_turned(j)
                    if j >= 1:
                        round_q(j - 1)

            @block.vector
            def _(dve):
                turn = Turns(dve, "dve_l0", "now16 next tiles tiles_before")
                for s in (scored, leaked, topped, centred, totalled, inverted, alpha_ready, var_ready, padded, inverse_ready, shift_ready,
                          var2_ready, padded2, inverse2_ready, shift2_ready):
                    dve.sem_inc(s, 1)
                for s in (weighed_ready, mixed_ready, sum_ready, stat_ready, stat2_ready, q_copied, q_low, kv_copied):
                    dve.sem_inc(s, LOT)

                def evacuate(j):
                    dve.wait_ge(q_done, turn.tile_before(j))
                    dve.wait_ge(out_free, turn.tile_before(j))
                    nc.vector.tensor_tensor(q_full[:, j, :], q_ps[:, j % 2, 0:H], bias_qkv[:, 0:H], ALU.add).then_inc(q_copied, 1)
                    dve.wait_ge(kv_done, turn.tile(j))
                    nc.vector.tensor_tensor(kv_out[:, j, :], kv_ps[:, j % 2, :], bias_qkv[:, H:3 * H], ALU.add).then_inc(kv_copied, 1)

                def low_q(j):
                    dve.wait_ge(q_high, turn.tile_before(j))
                    nc.vector.tensor_tensor(q_out[:, j, H:2 * H], q_full[:, j, :], q_out[:, j, 0:H], ALU.subtract).then_inc(q_low, 1)

                def alphas():
                    for j in range(LOT):
                        dve.wait_ge(src_landed[j], turn.now16)
                        dve.wait_ge(dst_landed[j], turn.now16)
                    nc.vector.tensor_tensor(score[:], by_src[:, :, H:H + HEADS], by_dst[:, :, H + HEADS:], ALU.add).then_inc(scored, 1)
                    dve.wait_ge(scored, turn.next)
                    nc.vector.scalar_tensor_tensor(out=leaky[:], in0=score[:], scalar=SLOPE, in1=score[:], op0=ALU.mult, op1=ALU.max).then_inc(leaked, 1)
                    dve.wait_ge(leaked, turn.next)
                    nc.vector.tensor_reduce(top_score[:], leaky[:], AX.X, ALU.max).then_inc(topped, 1)
                    dve.wait_ge(topped, turn.next)
                    nc.vector.tensor_tensor(score[:], leaky[:], top_score[:].unsqueeze(2).broadcast_to([P, LOT, HEADS]), ALU.subtract).then_inc(centred, 1)
                    dve.wait_ge(exped, turn.next)
                    nc.vector.tensor_reduce(total[:], prob[:], AX.X, ALU.add).then_inc(totalled, 1)
                    dve.wait_ge(totalled, turn.next)
                    nc.vector.reciprocal(top_score[:], total[:]).then_inc(inverted, 1)
                    dve.wait_ge(inverted, turn.next)
                    nc.vector.tensor_tensor(leaky[:], prob[:], top_score[:].unsqueeze(2).broadcast_to([P, LOT, HEADS]), ALU.mult).then_inc(alpha_ready, 1)
                    dve.wait_ge(alpha_ready, turn.next)

                def scale_and_shift(aggregated, added_eps, inverses, scales, shifts, meanwhile=()):
                    dve.wait_ge(aggregated, turn.next)
                    nc.vector.tensor_scalar(shift[:], mean_var[:, :, 1], EPS, None, ALU.add).then_inc(added_eps, 1)
                    dve.wait_ge(added_eps, turn.next)
                    nc.vector.reciprocal(inverse[:], shift[:]).then_inc(inverses, 1)
                    for j in meanwhile:
                        evacuate(j)
                    dve.wait_ge(scales, turn.next)
                    nc.vector.scalar_tensor_tensor(out=shift[:], in0=mean_var[:, :, 0], scalar=-1.0, in1=rstd[:], op0=ALU.mult, op1=ALU.mult).then_inc(shifts, 1)

                def mix(lot, lagged):
                    for i in range(LOT + 4):
                        if i < LOT:
                            nc.vector.tensor_tensor(weighed[:, i % 3, :].rearrange("p (h d) -> p h d", h=HEADS),
                                                    by_dst[:, i, 0:H].rearrange("p (h d) -> p h d", h=HEADS),
                                                    leaky[:, i, :].unsqueeze(2).broadcast_to([P, HEADS, DH]), ALU.mult).then_inc(weighed_ready, 1)
                        if 0 <= i - 1 < LOT:
                            j = i - 1
                            dve.wait_ge(weighed_ready, turn.tile(j))
                            nc.vector.tensor_reduce(mixed[:, j % 3, :], weighed[:, j % 3, :].rearrange("p (h d) -> p d h", h=HEADS), AX.X, ALU.add).then_inc(mixed_ready, 1)
                        if 0 <= i - 2 < LOT:
                            j = i - 2
                            dve.wait_ge(mixed_ready, turn.tile(j))
                            dve.wait_ge(x1_ready, turn.tile_before(j))
                            nc.vector.tensor_tensor(summed[:, j, :].rearrange("p (h d) -> p h d", h=HEADS),
                                                    x_sb[:, bass.ds(lot * LOT + j, 1), :].rearrange("p a (h d) -> p (a h) d", h=HEADS),
                                                    mixed[:, j % 3, :].unsqueeze(1).broadcast_to([P, HEADS, DH]), ALU.add).then_inc(sum_ready, 1)
                        if 0 <= i - 3 < LOT:
                            j = i - 3
                            dve.wait_ge(sum_ready, turn.tile(j))
                            nc.vector.bn_stats(stats[:, j, :], summed[:, j, :]).then_inc(stat_ready, 1)
                        if 0 <= i - 4 < LOT:
                            j = i - 4
                            reached = turn.reach(j)
                            dve.wait_ge(go, 1)
                            dve.wait_ge(stat_ready, reached)
                            last = nc.vector.bn_aggr(mean_var[:, j, :], stats[:, j, :])
                        if lagged and 0 <= i - 3 < LOT - 3:
                            evacuate(i - 3)
                    last.then_inc(var_ready, 1)

                def front(lot, lagged):
                    alphas()
                    dve.wait_ge(normed_ready, turn.tile_before(LOT - 1))
                    mix(lot, lagged)
                    scale_and_shift(var_ready, padded, inverse_ready, rstd_ready, shift_ready,
                                    meanwhile=range(LOT - 3, LOT - 2) if lagged else ())
                    if lagged:
                        evacuate(LOT - 2)
                    for i in range(LOT + 1):
                        if i < LOT:
                            reached = turn.reach(i)
                            dve.wait_ge(go, 1)
                            dve.wait_ge(x1_ready, reached)
                            nc.vector.bn_stats(stats[:, i, :], x_sb[:, bass.ds(lot * LOT + i, 1), :].rearrange("p a c -> p (a c)")).then_inc(stat2_ready, 1)
                        if i >= 1:
                            reached = turn.reach(i - 1)
                            dve.wait_ge(go, 1)
                            dve.wait_ge(stat2_ready, reached)
                            last = nc.vector.bn_aggr(mean_var[:, i - 1, :], stats[:, i - 1, :])
                        if lagged and i < LOT - 3:
                            low_q(i)
                    last.then_inc(var2_ready, 1)
                    if lagged:
                        low_q(LOT - 3)
                        evacuate(LOT - 1)
                        low_q(LOT - 2)
                        low_q(LOT - 1)
                    scale_and_shift(var2_ready, padded2, inverse2_ready, rstd2_ready, shift2_ready)
                    turn.step()

                front(0, False)
                with dve.Fori(1, LOTS) as lot:
                    front(lot, True)
                for j in range(LOT + 1):
                    if j < LOT:
                        evacuate(j)
                    if j >= 1:
                        low_q(j - 1)


def edge_stage(nc, shared):
    ident_bf, iota, steps, src_idx, dst_f, cut, window_f, walk, wd_hi_lo, wd_bias = (
        shared[n] for n in ("ident_bf", "iota", "steps", "src_idx", "dst_f", "cut", "window_f", "walk", "wd_hi_lo", "wd_bias"))
    q_tab, kv_tab, sum_tab, edge_attr_t, NP, N, E, BLOCKS = (
        shared[n] for n in ("q_tab", "kv_tab", "sum_tab", "edge_attr_t", "NP", "N", "E", "BLOCKS"))
    T, G = TURN_TILES, GROUP
    with nc.cleanup_on_exit(), ExitStack() as ctx:
        scope = Scope(nc, ctx, "e_")
        sb, psum, sem, sems = scope.sb, scope.psum, scope.sem, scope.sems

        attr = sb("attr", [P, 2, SPAN], F32)
        high = sb("high", [P, 2, SPAN], F32R)
        low = sb("low", [P, 2, SPAN], F32R)
        idx = sb("idx", [P, T], I32)
        kv = sb("kv", [P, T, 2 * H], F32)
        gates = sb("gates", [P, T, 2 * H], F32)
        q_win = sb("q_win", [P, 2 * H], F32R)
        place = sb("place", [P, BLOCK_TILES], F32)
        hot = sb("hot", [P, BLOCK_TURNS, T, P], BF16)
        hot_t = sb("hot_t", [P, T, P], F32R)
        weighed_hot = sb("weighed_hot", [P, T, P], F32)
        gated = sb("gated", [P, BLOCK_TURNS, T, 2 * H], F32)
        dot = sb("dot", [P, 2, G], F32)
        silu_dot = sb("silu_dot", [P, 2, G], F32)
        cut_now = sb("cut_now", [P, 2, G], F32)
        attn = sb("attn", [P, 2, G], F32)
        sums = sb("sums", [P, H], F32)

        gate_ps = [psum(f"gate_ps{s}", [P, 2 * H], F32) for s in range(2)]
        q_ps = psum("q_ps", [P, T, H], F32)
        hot_ps = psum("hot_ps", [P, G, P], BF16)
        sum_ps = psum("sum_ps", [P, H], F32)

        attr_top, attr_bottom = sems("attr_top", 2), sems("attr_bottom", 2)
        q_landed = sem("q_landed")
        kv_landed = sems("kv_landed", T)
        added = sem("added")
        high_ready, low_ready = sems("high_ready", 2), sems("low_ready", 2)
        idx_ready, place_ready = sems("idx_ready", 2), sem("place_ready")
        gate_done, gate_ready, q_done = (sems(n, T) for n in ("gate_done", "gate_ready", "q_done"))
        hot_ready, hot_turned, hot_t_ready = (sems(n, 2) for n in ("hot_ready", "hot_turned", "hot_t_ready"))
        gated_ready, dotted = sems("gated_ready", T // 2), sems("dotted", T)
        silu_2 = sems("silu_2", 2)
        attn_2 = sems("attn_2", 2)
        weighed_2 = sems("weighed_2", T)
        summed = sems("summed", T)
        sums_2 = sem("sums_2")
        go = sem("go")
        zeroed, dummy_gathers, ready = sem("zeroed"), sem("dummy_gathers"), sem("ready")

        def visits(eng, t):
            return eng.value_load(walk[0:1, 0, bass.ds(t, 1)], min_val=1, max_val=-(-N // P))

        def window_row(eng, first, r):
            return nc.s_assert_within(first + r * P, 0, NP - P,
                                      skip_runtime_bounds_check_because="a window starts at or below the largest dst")

        def columns(half):
            return half.rearrange("r (p j) -> r j p", j=G)

        def tiled(half):
            return half.rearrange("r (j p) -> r j p", j=G)

        with nc.Block() as block:
            @block.sync
            def _(sp):
                turn = Turns(sp, "sp_e", "now")

                def load_attr(g, first):
                    sp.wait_ge(go, 1)
                    sp.wait_ge(high_ready[g], turn.now)
                    sp.wait_ge(low_ready[g], turn.now)
                    part = edge_attr_t[:, bass.ds(first, SPAN)]
                    sp.dma_start(attr[0:R, g, :], part).then_inc(attr_top[g], 16)
                    sp.dma_start(attr[R:P, g, :], part).then_inc(attr_bottom[g], 16)

                sp.wait_ge(zeroed, 1)
                with sp.Fori(0, BLOCKS) as t:
                    n = visits(sp, t)
                    node = sp.value_load(walk[0:1, 1, bass.ds(t, 1)], min_val=0, max_val=N - 1)
                    edge = sp.value_load(walk[0:1, 2, bass.ds(t, 1)], min_val=0, max_val=E - BLOCK)
                    with sp.Fori(0, n) as r:
                        for half in range(BLOCK_TURNS):
                            load_attr(0, edge + half * T * P)
                            load_attr(1, edge + half * T * P + SPAN)
                            if half == 0:
                                sp.wait_ge(go, 1)
                                sp.wait_ge(q_done[T - 1], turn.now)
                                sp.dma_start(q_win[:].bitcast(F32), q_tab[bass.ds(window_row(sp, node, r), P), :]).then_inc(q_landed, 16)
                            turn.step()
                load_attr(0, 0)

            @block.gpsimd
            def _(pool):
                turn = Turns(pool, "pool_e", "now next now16")
                visit = Turns(pool, "pool_e_visit", "next next16")
                pool.sem_inc(go, 1)
                row_before = pool.alloc_register("pool_row_before")
                pool.reg_mov(row_before, 0)
                for s in idx_ready:
                    pool.sem_inc(s, 1)

                def gather(k):
                    pool.indirect_dma_start(kv[:, k, :], None, kv_tab,
                                            bass.IndirectOffsetOnAxis(ap=idx[:, k:k + 1], axis=0)).then_inc(kv_landed[k], 16)

                def gather_group(g, tile):
                    tiles = range(g * G, (g + 1) * G)
                    for k in tiles:
                        pool.wait_ge(kv_landed[k], turn.now16)
                    nc.gpsimd.tensor_copy(idx[:, g * G:(g + 1) * G], src_idx[:, bass.ds(tile, G)]).then_inc(idx_ready[g], 1)
                    pool.wait_ge(go, 1)
                    pool.wait_ge(idx_ready[g], turn.next)
                    for k in tiles:
                        pool.wait_ge(go, 1)
                        pool.wait_ge(gated_ready[k // 2], turn.now)
                        gather(k)

                def add_sums():
                    pool.wait_ge(go, 1)
                    pool.wait_ge(sums_2, visit.next)
                    row = nc.s_assert_within(pool.snap(row_before), 0, NP - P,
                                             skip_runtime_bounds_check_because="it is a window's first row")
                    pool.dma_start(sum_tab[bass.ds(row, P), :], sums[:], accum_op=ALU.add).then_inc(added, 16)

                nc.gpsimd.tensor_copy(idx[:], src_idx[:, 0:T]).then_inc(dummy_gathers, 1)
                nc.gpsimd.memset(low[:].bitcast(F32), 0.0).then_inc(dummy_gathers, 1)
                pool.wait_ge(dummy_gathers, 2)
                nc.gpsimd.memset(low[64:65, :, :].bitcast(F32), 1.0).then_inc(dummy_gathers, 1)
                pool.wait_ge(dummy_gathers, 3)
                nc.gpsimd.memset(low[96:97, :, :].bitcast(F32), 1.0).then_inc(zeroed, 1)
                pool.wait_ge(zeroed, 1)
                for k in range(T):
                    gather(k)
                pool.wait_ge(ready, 1)
                pool.dma_start(sum_tab[0:P, :], sums[:], accum_op=ALU.add).then_inc(added, 16)
                with pool.Fori(0, BLOCKS) as t:
                    n = visits(pool, t)
                    node = pool.value_load(walk[0:1, 1, bass.ds(t, 1)], min_val=0, max_val=N - 1)
                    with pool.Fori(0, n) as r:
                        for half in range(BLOCK_TURNS):
                            gather_group(0, t * BLOCK_TILES + half * T)
                            gather_group(1, t * BLOCK_TILES + half * T + G)
                            if half == 1:
                                add_sums()
                            turn.step()
                        pool.reg_mov(row_before, window_row(pool, node, r))
                        visit.step()
                add_sums()
                pool.wait_ge(added, visit.next16)
                for k in range(T):
                    pool.wait_ge(kv_landed[k], turn.now16)

            @block.tensor
            def _(pe):
                turn = Turns(pe, "pe_e", "now next after")
                visit = Turns(pe, "pe_e_visit", "next now16")
                for group in (gate_done, q_done, hot_turned):
                    for s in group:
                        pe.sem_inc(s, 1)
                for s in summed:
                    pe.sem_inc(s, 1)
                for s in summed[1:]:
                    pe.sem_inc(s, 1)

                def segment_sum(k, half):
                    pe.wait_ge(weighed_2[k], turn.next)
                    pe.wait_ge(gated_ready[k // 2], turn.now)
                    if half == 1 and k == 0:
                        pe.wait_ge(sums_2, visit.next)
                    nc.tensor.matmul(sum_ps[:], weighed_hot[:, k, :], gated[:, 1 - half, k, H:2 * H], start=(half == 1 and k == 0), stop=(half == 0 and k == T - 1)).then_inc(summed[k], 1)

                def turn_hot(g, half):
                    pe.wait_ge(hot_ready[g], turn.next)
                    pe.wait_ge(hot_t_ready[1 - g], turn.next if g else turn.now)
                    for k in range(g * G, g * G + G):
                        last = nc.tensor.transpose(hot_ps[:, k % G, :], hot[:, half, k, :], ident_bf[:])
                    last.then_inc(hot_turned[g], 1)

                def gate(k, ready, before):
                    g = k // G
                    if k % G == 0:
                        pe.wait_ge(high_ready[g], ready)
                        pe.wait_ge(low_ready[g], ready)
                    if k >= 2:
                        pe.wait_ge(gate_ready[k - 2], ready)
                    else:
                        pe.wait_ge(gate_ready[T - 2 + k], before)
                    cols = slice((k % G) * P, (k % G + 1) * P)
                    nc.tensor.matmul(gate_ps[k % 2][:], high[:, g, cols], wd_hi_lo[:], start=True, stop=False)
                    nc.tensor.matmul(gate_ps[k % 2][:], low[:, g, cols], wd_bias[:], start=False, stop=True).then_inc(gate_done[k], 1)

                def gather_q(k):
                    if k == 0:
                        pe.wait_ge(q_landed, visit.now16)
                    if k % G == 0:
                        pe.wait_ge(hot_t_ready[k // G], turn.next)
                    if k % 2 == 0:
                        pe.wait_ge(dotted[k + 1], turn.now)
                    nc.tensor.matmul(q_ps[:, k, :], hot_t[:, k, :], q_win[:, 0:H], start=True, stop=False)
                    nc.tensor.matmul(q_ps[:, k, :], hot_t[:, k, :], q_win[:, H:2 * H], start=False, stop=True).then_inc(q_done[k], 1)

                pe.wait_ge(ready, 1)
                nc.tensor.matmul(sum_ps[:], weighed_hot[:, 0, :], gated[:, 0, 0, H:2 * H], start=True, stop=False).then_inc(summed[0], 1)
                for k in range(2):
                    gate(k, turn.next, turn.now)
                with pe.Fori(0, BLOCKS) as t:
                    n = visits(pe, t)
                    with pe.Fori(0, n):
                        for half in range(BLOCK_TURNS):
                            for g in range(2):
                                k = g * G
                                turn_hot(g, half)
                                gate(k + 2, turn.next, turn.now)
                                gather_q(k)
                                gather_q(k + 1)
                                gate(k + 3, turn.next, turn.now)
                                gather_q(k + 2)
                                gather_q(k + 3)
                                for j in range(2):
                                    if g == 0:
                                        gate(G + j, turn.next, turn.now)
                                    else:
                                        gate(j, turn.after, turn.next)
                                for j in range(G):
                                    segment_sum(k + j, half)
                            turn.step()
                        visit.step()
                for k in range(T):
                    segment_sum(k, 0)

            @block.scalar
            def _(act):
                turn = Turns(act, "act_e", "now next after now16 next16")
                visit = Turns(act, "act_e_visit", "now16")
                for group in (hot_t_ready, gate_ready, high_ready, silu_2, [sums_2], weighed_2):
                    for s in group:
                        act.sem_inc(s, 1)

                def round_attr(g, landed, used):
                    act.wait_ge(attr_top[g], landed)
                    act.wait_ge(attr_bottom[g], landed)
                    act.wait_ge(gate_done[G * g + G - 1], used)
                    nc.scalar.copy(tiled(high[:, g, :]), columns(attr[:, g, :])).then_inc(high_ready[g], 1)

                def weigh(k, half):
                    act.wait_ge(attn_2[k // G], turn.next)
                    act.wait_ge(summed[k], turn.next)
                    nc.scalar.activation(weighed_hot[:, k, :], hot[:, 1 - half, k, :], ACT.Copy, scale=attn[:, k // G, k % G:k % G + 1]).then_inc(weighed_2[k], 1)

                def tile(k):
                    act.wait_ge(gate_done[k], turn.next)
                    act.wait_ge(gated_ready[k // 2], turn.now)
                    nc.scalar.activation(gates[:, k, :], gate_ps[k % 2][:], ACT.Silu).then_inc(gate_ready[k], 1)

                def copy_hot(g):
                    act.wait_ge(hot_turned[g], turn.next)
                    act.wait_ge(q_done[g * G + G - 1], turn.now)
                    nc.scalar.copy(hot_t[:, g * G:(g + 1) * G, :], hot_ps[:]).then_inc(hot_t_ready[g], 1)

                def silu(g):
                    act.wait_ge(dotted[g * G + G - 1], turn.now)
                    act.wait_ge(attn_2[g], turn.now)
                    nc.scalar.activation(silu_dot[:, g, :], dot[:, g, :], ACT.Silu).then_inc(silu_2[g], 1)

                def take_sums(done):
                    act.wait_ge(summed[T - 1], done)
                    act.wait_ge(added, visit.now16)
                    nc.scalar.copy(sums[:], sum_ps[:]).then_inc(sums_2, 1)

                act.wait_ge(ready, 1)
                nc.scalar.preload_act_table(ACT.Silu)
                round_attr(0, turn.now16, turn.now)
                with act.Fori(0, BLOCKS) as t:
                    n = visits(act, t)
                    with act.Fori(0, n):
                        for half in range(BLOCK_TURNS):
                            for g in range(2):
                                k = g * G
                                if g == 0:
                                    round_attr(1, turn.now16, turn.now)
                                else:
                                    round_attr(0, turn.next16, turn.next)
                                silu(g)
                                tile(k)
                                tile(k + 1)
                                copy_hot(g)
                                if half == 1 and g == 0:
                                    take_sums(turn.next)
                                tile(k + 2)
                                weigh(k, half)
                                weigh(k + 1, half)
                                tile(k + 3)
                                weigh(k + 2, half)
                                weigh(k + 3, half)
                            turn.step()
                        visit.step()
                for g in range(2):
                    silu(g)
                    for k in range(g * G, (g + 1) * G):
                        weigh(k, 0)
                take_sums(turn.after)

            @block.vector
            def _(dve):
                turn = Turns(dve, "dve_e", "now next after now16 next16")
                visit = Turns(dve, "dve_e_visit", "next")
                for group in ([place_ready], low_ready, hot_ready, attn_2, gated_ready[:G // 2], dotted[:2]):
                    for s in group:
                        dve.sem_inc(s, 1)
                for t in (hot, attn, dot, cut_now, gates, gated, weighed_hot, sums, q_ps):
                    last = nc.vector.memset(t[:], 0.0)
                last.then_inc(ready, 1)

                def gated_rows(k, half):
                    done = turn.now if k >= G else turn.next
                    for tile in (k, k + 1):
                        dve.wait_ge(kv_landed[tile], turn.now16 if k >= G else turn.next16)
                        dve.wait_ge(gate_ready[tile], done)
                        dve.wait_ge(summed[tile], done)
                    nc.vector.tensor_tensor(gated[:, 1 - half if k >= G else half, k:k + 2, :], kv[:, k:k + 2, :], gates[:, k:k + 2, :],
                                            ALU.mult).then_inc(gated_ready[k // 2], 1)

                def dot_rows(k, half):
                    before = k >= 2
                    g, done = k // G, turn.now if before else turn.next
                    dve.wait_ge(q_done[k + 1 - k % 2], done)
                    dve.wait_ge(gated_ready[k // 2], done)
                    if k % G == 0:
                        dve.wait_ge(silu_2[g], turn.now if g else turn.next)
                    rows = gated[:, 1 - half if before else half, k, 0:H]
                    nc.vector.tensor_tensor_reduce(rows, rows, q_ps[:, k, :], 1.0, 0.0,
                                                   ALU.mult, ALU.add, dot[:, g, k % G:k % G + 1]).then_inc(dotted[k], 1)

                def attend(g):
                    dve.wait_ge(silu_2[g], turn.next)
                    for k in range(G):
                        dve.wait_ge(weighed_2[g * G + k], turn.now)
                    nc.vector.tensor_tensor(attn[:, g, :], silu_dot[:, g, :], cut_now[:, g, :], ALU.mult).then_inc(attn_2[g], 1)

                def one_hot(g, half):
                    tiles = slice(g * G, (g + 1) * G)
                    places = slice(half * T + g * G, half * T + (g + 1) * G)
                    for k in range(g * G, (g + 1) * G):
                        dve.wait_ge(weighed_2[k], turn.now)
                    nc.vector.tensor_tensor(hot[:, half, tiles, :], iota[:].unsqueeze(1).broadcast_to([P, G, P]),
                                            place[:, places].unsqueeze(2).broadcast_to([P, G, P]), ALU.is_equal).then_inc(hot_ready[g], 1)

                def low_attr(g, ready, used):
                    dve.wait_ge(high_ready[g], ready)
                    dve.wait_ge(gate_done[G * g + G - 1], used)
                    nc.vector.tensor_tensor(tiled(low[0:R, g, :]), columns(attr[0:R, g, :]), tiled(high[0:R, g, :]), ALU.subtract).then_inc(low_ready[g], 1)

                dve.wait_ge(zeroed, 1)
                low_attr(0, turn.next, turn.now)
                with dve.Fori(0, BLOCKS) as t:
                    n = visits(dve, t)
                    with dve.Fori(0, n) as r:
                        dve.wait_ge(hot_ready[1], turn.now)
                        nc.vector.tensor_scalar(place[:], dst_f[:, bass.ds(t * BLOCK_TILES, BLOCK_TILES)], window_f[:, bass.ds(t, 1)],
                                                steps[:, bass.ds(r, 1)], ALU.subtract, ALU.subtract).then_inc(place_ready, 1)
                        for half in range(BLOCK_TURNS):
                            dot_rows(2, half)
                            dot_rows(3, half)
                            gated_rows(4, half)
                            if half == 0:
                                dve.wait_ge(place_ready, visit.next)
                            one_hot(0, half)
                            dot_rows(4, half)
                            dot_rows(5, half)
                            gated_rows(6, half)
                            attend(0)
                            low_attr(1, turn.next, turn.now)
                            dot_rows(6, half)
                            dot_rows(7, half)
                            gated_rows(0, half)
                            one_hot(1, half)
                            dot_rows(0, half)
                            dot_rows(1, half)
                            attend(1)
                            low_attr(0, turn.after, turn.next)
                            dve.wait_ge(attn_2[0], turn.next)
                            dve.wait_ge(attn_2[1], turn.next)
                            nc.vector.tensor_copy(cut_now[:].rearrange("p g j -> p (g j)"), cut[:, bass.ds(t * BLOCK_TILES + half * T, T)])
                            gated_rows(2, half)
                            turn.step()
                        visit.step()
                for k in (2, 3):
                    dot_rows(k, 0)
                for k in range(G, T, 2):
                    gated_rows(k, 0)
                attend(0)
                for k in range(G, T):
                    dot_rows(k, 0)
                attend(1)


def output_stage(nc, shared):
    x_sb, ident, wo, bo_rep, sum_tab, out, TILES, LOTS, N = (
        shared[n] for n in ("x_sb", "ident", "wo", "bo_rep", "sum_tab", "out", "TILES", "LOTS", "N"))
    with nc.cleanup_on_exit(), ExitStack() as ctx:
        scope = Scope(nc, ctx, "o_")
        sb, psum, sem, sems = scope.sb, scope.psum, scope.sem, scope.sems
        sums = sb("sums", [P, LOT, H], F32)
        sums_t = sb("sums_t", [P, 2, 2 * P], F32)
        summed = sb("summed", [P, LOT, H], F32)
        stats = sb("stats", [P, LOT, 6], F32)
        mean_var = sb("mean_var", [P, LOT, 2], F32)
        padded_var = sb("padded_var", [P, LOT], F32)
        inverse = sb("inverse", [P, LOT], F32)
        rstd = sb("rstd", [P, LOT], F32)
        shift = sb("shift", [P, LOT], F32)
        result = sb("result", [P, LOT, H], F32)
        turned_ps = psum("turned_ps", [P, 2, 512], F32)
        out_ps = psum("out_ps", [P, 2, 512], F32)

        landed, stored, go = sems("landed", LOT), sems("stored", LOT), sem("go")
        turned, turned_copied, done, biased, sum_ready, stat_ready, result_ready, result_free = (
            sem(n) for n in ("turned", "turned_copied", "done", "biased", "sum_ready", "stat_ready", "result_ready", "result_free"))
        var_ready, padded, inverse_ready, rstd_ready, shift_ready = (
            sem(n) for n in ("var_ready", "padded", "inverse_ready", "rstd_ready", "shift_ready"))

        with nc.Block() as block:
            @block.sync
            def _(sp):
                turn = Turns(sp, "sp_o", "tiles_before")
                with sp.Fori(0, LOTS) as lot:
                    for j in range(LOT):
                        reached = turn.reach_before(j)
                        sp.wait_ge(go, 1)
                        sp.wait_ge(turned, reached)
                        sp.dma_start(sums[:, j, :], sum_tab[bass.ds(lot * (LOT * P) + j * P, P), :]).then_inc(landed[j], 16)
                    turn.step()

            @block.gpsimd
            def _(pool):
                turn = Turns(pool, "pool_o", "now16 tiles")
                pool.sem_inc(go, 1)
                pool.sem_inc(result_free, 2 * LOT)

                def store(row, j, rows):
                    reached = turn.reach(j)
                    pool.wait_ge(go, 1)
                    pool.wait_ge(result_ready, reached)
                    pool.dma_start(out[row, :], result[0:rows, j, :]).then_inc(stored[j], 16)

                def release(j):
                    pool.wait_ge(stored[j], turn.now16)
                    pool.sem_inc(result_free, 1)

                with pool.Fori(0, LOTS - 1) as lot:
                    for j in range(LOT):
                        store(bass.ds(lot * (LOT * P) + j * P, P), j, P)
                        if j >= 3:
                            release(j - 3)
                    for j in range(LOT - 3, LOT):
                        release(j)
                    turn.step()
                for j in range(LOT):
                    first = ((LOTS - 1) * LOT + j) * P
                    if first < N:
                        rows = min(P, N - first)
                        store(slice(first, first + rows), j, rows)
                for j in range(LOT):
                    if ((LOTS - 1) * LOT + j) * P < N:
                        pool.wait_ge(stored[j], 16 * LOTS)

            @block.tensor
            def _(pe):
                turn = Turns(pe, "pe_o", "now16 tiles tiles_before")
                pe.sem_inc(turned, LOT)
                pe.sem_inc(done, LOT)

                def turn_tile(j):
                    pe.wait_ge(landed[j], turn.now16)
                    wait_slot(pe, turned_copied, j, turn)
                    for k in range(2):
                        last = nc.tensor.transpose(turned_ps[:, j % 2, k * P:(k + 1) * P], sums[:, j, k * P:(k + 1) * P], ident[:])
                    last.then_inc(turned, 1)

                with pe.Fori(0, LOTS):
                    turn_tile(0)
                    for j in range(LOT):
                        if j + 1 < LOT:
                            turn_tile(j + 1)
                        pe.wait_ge(turned_copied, turn.tile(j))
                        wait_slot(pe, biased, j, turn)
                        for k in range(2):
                            last = nc.tensor.matmul(out_ps[:, j % 2, 0:H], sums_t[:, j % 2, k * P:(k + 1) * P], wo[:, k, :],
                                                    start=(k == 0), stop=(k == 1))
                        last.then_inc(done, 1)
                    turn.step()

            @block.scalar
            def _(act):
                turn = Turns(act, "act_o", "now next tiles tiles_before")
                act.sem_inc(turned_copied, LOT)
                act.sem_inc(result_ready, LOT)
                act.sem_inc(rstd_ready, 1)
                nc.scalar.preload_act_table(ACT.Sqrt)

                def copy_turned(j):
                    act.wait_ge(turned, turn.tile(j))
                    wait_slot(act, done, j, turn)
                    nc.scalar.copy(sums_t[:, j % 2, :], turned_ps[:, j % 2, 0:H]).then_inc(turned_copied, 1)

                def root():
                    act.wait_ge(inverse_ready, turn.next)
                    nc.scalar.activation(rstd[:], inverse[:], ACT.Sqrt).then_inc(rstd_ready, 1)

                def norm(j):
                    act.wait_ge(shift_ready, turn.now)
                    act.wait_ge(result_free, turn.tile_before(j))
                    nc.scalar.activation(result[:, j, :], summed[:, j, :], ACT.Identity, bias=shift[:, j:j + 1],
                                         scale=rstd[:, j:j + 1]).then_inc(result_ready, 1)

                for j in range(LOT):
                    copy_turned(j)
                root()
                turn.step()
                with act.Fori(1, LOTS):
                    for j in range(LOT):
                        copy_turned(j)
                        norm(j)
                    root()
                    turn.step()
                for j in range(LOT):
                    norm(j)

            @block.vector
            def _(dve):
                turn = Turns(dve, "dve_o", "next tiles tiles_before")
                for s in (biased, sum_ready, stat_ready):
                    dve.sem_inc(s, LOT)
                for s in (var_ready, padded, inverse_ready, shift_ready):
                    dve.sem_inc(s, 1)
                with dve.Fori(0, LOTS) as lot:
                    for i in range(LOT + 3):
                        if i < LOT:
                            dve.wait_ge(done, turn.tile(i))
                            dve.wait_ge(result_ready, turn.tile_before(i))
                            nc.vector.tensor_tensor(summed[:, i, :], out_ps[:, i % 2, 0:H], bo_rep[:], ALU.add).then_inc(biased, 1)
                        if 0 <= i - 1 < LOT:
                            j = i - 1
                            dve.wait_ge(biased, turn.tile(j))
                            nc.vector.scalar_tensor_tensor(out=summed[:, j, :], in0=x_sb[:, bass.ds(lot * LOT + j, 1), :].rearrange("p a c -> p (a c)"),
                                                           scalar=2.0, in1=summed[:, j, :], op0=ALU.mult, op1=ALU.add).then_inc(sum_ready, 1)
                        if 0 <= i - 2 < LOT:
                            j = i - 2
                            dve.wait_ge(sum_ready, turn.tile(j))
                            nc.vector.bn_stats(stats[:, j, :], summed[:, j, :]).then_inc(stat_ready, 1)
                        if 0 <= i - 3 < LOT:
                            j = i - 3
                            reached = turn.reach(j)
                            dve.wait_ge(go, 1)
                            dve.wait_ge(stat_ready, reached)
                            last = nc.vector.bn_aggr(mean_var[:, j, :], stats[:, j, :])
                    last.then_inc(var_ready, 1)
                    dve.wait_ge(var_ready, turn.next)
                    nc.vector.tensor_scalar(padded_var[:], mean_var[:, :, 1], EPS, None, ALU.add).then_inc(padded, 1)
                    dve.wait_ge(padded, turn.next)
                    nc.vector.reciprocal(inverse[:], padded_var[:]).then_inc(inverse_ready, 1)
                    dve.wait_ge(rstd_ready, turn.next)
                    nc.vector.scalar_tensor_tensor(out=shift[:], in0=mean_var[:, :, 0], scalar=-1.0, in1=rstd[:],
                                                   op0=ALU.mult, op1=ALU.mult).then_inc(shift_ready, 1)
                    turn.step()


def kernel(x, src, dst, edge_attr_64, edge_weight, L0_gnn_weight, L0_gnn_attn_l, L0_gnn_attn_r, L1_gnn_ln_g, L1_gnn_ln_b,
           L1_gnn_Wq, L1_gnn_bq, L1_gnn_Wk, L1_gnn_bk, L1_gnn_Wv, L1_gnn_bv, L1_gnn_Wo, L1_gnn_bo,
           L1_gnn_Wdk, L1_gnn_bdk, L1_gnn_Wdv, L1_gnn_bdv):
    import concourse.bacc as bacc
    import numpy as np
    from concourse.bass_utils import run_bass_kernel_spmd

    x = np.ascontiguousarray(x)
    n_nodes, n_edges = x.shape[0], len(src)
    blocks = -(-n_edges // BLOCK)
    tiles = -(-n_nodes // (P * LOT)) * LOT

    def by_tile(values):
        values = np.asarray(values)
        whole = values[:(blocks - 1) * BLOCK].reshape(blocks - 1, BLOCK // SPAN, P, GROUP)
        last = values[n_edges - BLOCK:].reshape(1, BLOCK // SPAN, P, GROUP)
        return np.ascontiguousarray(np.concatenate([whole, last]).transpose(2, 0, 1, 3).reshape(P, blocks * BLOCK_TILES))

    def first_edges(values):
        return np.ascontiguousarray(np.asarray(values)[:tiles * P].reshape(tiles, P).T)

    def columns(values):
        return np.ascontiguousarray(np.asarray(values).reshape(2, P).T)

    def beside(*weights):
        return np.ascontiguousarray(np.concatenate([np.asarray(w).T for w in weights], axis=1))

    def joined(*biases):
        return np.concatenate([np.asarray(b) for b in biases])

    arrays = {
        "x": x, "src_tiles": by_tile(src), "dst_tiles": by_tile(dst), "edge_weight_tiles": by_tile(edge_weight),
        "src_first": first_edges(src), "dst_first": first_edges(dst),
        "edge_attr_t": np.ascontiguousarray(np.asarray(edge_attr_64).T),
        "weight": np.ascontiguousarray(L0_gnn_weight), "attn_l": np.ascontiguousarray(L0_gnn_attn_l),
        "attn_r": np.ascontiguousarray(L0_gnn_attn_r), "ln_g": columns(L1_gnn_ln_g), "ln_b": columns(L1_gnn_ln_b),
        "wqkv_t": beside(L1_gnn_Wq, L1_gnn_Wk, L1_gnn_Wv), "bqkv": joined(L1_gnn_bq, L1_gnn_bk, L1_gnn_bv),
        "wo_t": beside(L1_gnn_Wo), "bo": np.ascontiguousarray(L1_gnn_bo),
        "wd_t": beside(L1_gnn_Wdk, L1_gnn_Wdv), "bd": joined(L1_gnn_bdk, L1_gnn_bdv),
    }
    nc = bacc.Bacc("TRN2", target_bir_lowering=False, num_devices=1)
    args = {n: nc.dram_tensor(f"{n}_dram", v.shape, mybir.dt.from_np(v.dtype), kind="ExternalInput").ap() for n, v in arrays.items()}
    out = nc.dram_tensor("out_dram", x.shape, F32, kind="ExternalOutput").ap()
    gnn_kernel(nc, **args, out=out)
    result = run_bass_kernel_spmd(nc, [{f"{n}_dram": v for n, v in arrays.items()}], core_ids=[0])
    return result.results[0]["out_dram"]
```
